# Optimizing a Trainium2 kernel written in Bass

```python
import numpy as np
import jax
import jax.numpy as jnp

def _softmax(x, axis=-1):
    return jax.nn.softmax(x, axis=axis)

def _gelu(x):
    return jax.nn.gelu(x, approximate=True)

def _silu(x):
    return jax.nn.silu(x)

def _sigmoid(x):
    return jax.nn.sigmoid(x)

def _layernorm(x, axis=-1, eps=1e-05):
    m = jnp.mean(x, axis=axis, keepdims=True)
    v = jnp.var(x, axis=axis, keepdims=True)
    return (x - m) / jnp.sqrt(v + eps)

def _scatter_add(tgt, idx, src, axis=0):
    return tgt.at[idx].add(src)

def _segment_sum(src, seg, n):
    return jax.ops.segment_sum(src, seg, n)
kernel_name = 'mk_adaln_ffn_d1_seqx_r4_7b7b92'

def setup_inputs(seed: int=0):
    np.random.seed(seed)
    _w = jnp.asarray

    def _rec_inputs():
        import jax
        import jax.numpy as jnp
        _rk = jax.random.key(seed)
        x = -0.000125 + 0.9999 * jax.random.normal(jax.random.fold_in(_rk, 1), (8, 256, 1024), jnp.float32)
        _lenS = 256 - jax.random.randint(jax.random.fold_in(_rk, 7), (8,), 0, max(1, 256 // 4) + 1, jnp.int32)
        _lenS2 = 256 - jax.random.randint(jax.random.fold_in(_rk, 8), (8,), 0, max(1, 256 // 4) + 1, jnp.int32)
        itok_B_3_7 = jax.random.randint(jax.random.fold_in(_rk, 11), (8,), 3, 8, jnp.int32)
        return (x, itok_B_3_7)
    x, itok_B_3_7 = _rec_inputs()

    def _L0_cond_setup():
        import jax, jax.numpy as jnp
        import numpy as np
        MAX_LORAS, OUT, IN = (8, 1024, 1024)
        B, S = (4, 512)
        key = jax.random.key(seed)
        k1, k2, k3 = jax.random.split(key, 3)
        x = jax.random.normal(k1, (B, S, IN), dtype=jnp.float32)
        weight = jax.random.normal(k2, (MAX_LORAS, OUT, IN), dtype=jnp.float32) * 0.02
        adapter_ids = jax.random.randint(k3, (B,), 0, MAX_LORAS, dtype=jnp.int32)
        return {'x': x, 'weight': weight, 'adapter_ids': adapter_ids}
    _L0_cond_all = _L0_cond_setup()
    _L0_cond_in = {k: v for k, v in _L0_cond_all.items() if k in ('weight',)}
    del _L0_cond_all

    def _L0_ffn_setup():
        import jax, jax.numpy as jnp
        import numpy as np
        SCALING = 32.0 / 16.0
        key = jax.random.key(seed)
        ks = jax.random.split(key, 7)
        B, T, D, O, R, E = (4, 512, 1024, 1024, 16, 8)
        x = jax.random.normal(ks[0], (B, T, D), dtype=jnp.float32)
        base_W = jax.random.normal(ks[1], (O, D), dtype=jnp.float32) * D ** (-0.5)
        base_b = jax.random.normal(ks[2], (O,), dtype=jnp.float32) * 0.01
        router_W = jax.random.normal(ks[3], (2 * E - 1, D), dtype=jnp.float32) * D ** (-0.5)
        router_b = jax.random.normal(ks[4], (2 * E - 1,), dtype=jnp.float32) * 0.01
        A = jax.random.normal(ks[5], (E, R, D), dtype=jnp.float32) * D ** (-0.5)
        Bm = jax.random.normal(ks[6], (E, O, R), dtype=jnp.float32) * R ** (-0.5)
        assigned_idx = 0
        others = [i for i in range(E) if i != assigned_idx]
        expert_map = jnp.array([assigned_idx] * E + others, dtype=jnp.int32)
        return {'x': x, 'base_W': base_W, 'base_b': base_b, 'router_W': router_W, 'router_b': router_b, 'A': A, 'B': Bm, 'expert_map': expert_map}
    _L0_ffn_all = _L0_ffn_setup()
    _L0_ffn_in = {k: v for k, v in _L0_ffn_all.items() if k in ('base_W', 'base_b', 'router_W', 'router_b', 'A', 'B', 'expert_map')}
    del _L0_ffn_all
    return {'x': x, 'itok_B_3_7': itok_B_3_7, 'L0_cond_weight': _L0_cond_in['weight'], 'L0_ffn_base_W': _L0_ffn_in['base_W'], 'L0_ffn_base_b': _L0_ffn_in['base_b'], 'L0_ffn_router_W': _L0_ffn_in['router_W'], 'L0_ffn_router_b': _L0_ffn_in['router_b'], 'L0_ffn_A': _L0_ffn_in['A'], 'L0_ffn_B': _L0_ffn_in['B'], 'L0_ffn_expert_map': _L0_ffn_in['expert_map']}

def reference(x, itok_B_3_7, L0_cond_weight, L0_ffn_base_W, L0_ffn_base_b, L0_ffn_router_W, L0_ffn_router_b, L0_ffn_A, L0_ffn_B, L0_ffn_expert_map):
    import jax
    import jax.numpy as jnp

    def _L0_cond_ref(x, weight, adapter_ids):
        import jax, jax.numpy as jnp
        import numpy as np
        MAX_LORAS, OUT, IN = (8, 1024, 1024)
        B, S = (4, 512)
        w = weight[adapter_ids]
        return jnp.einsum('bsi,boi->bso', x, w)

    def _L0_ffn_ref(x, base_W, base_b, router_W, router_b, A, B, expert_map):
        import jax, jax.numpy as jnp
        import numpy as np
        SCALING = 32.0 / 16.0
        E = A.shape[0]
        base_out = jnp.einsum('btd,od->bto', x, base_W) + base_b
        logits = jnp.einsum('btd,nd->btn', x, router_W) + router_b
        probs = jax.nn.softmax(logits, axis=-1)
        topk_p, topk_i = jax.lax.top_k(probs, E)
        mapped = expert_map[topk_i]
        onehot = (mapped[..., None] == jnp.arange(E)).astype(x.dtype)
        w = jnp.einsum('btk,btke->bte', topk_p, onehot)
        h = jnp.einsum('btd,erd->bter', x, A)
        lora = jnp.einsum('bter,eor->bto', h * w[..., None], B) * SCALING
        return base_out + lora
    x = x + _L0_ffn_ref(_L0_cond_ref(x, L0_cond_weight, itok_B_3_7), L0_ffn_base_W, L0_ffn_base_b, L0_ffn_router_W, L0_ffn_router_b, L0_ffn_A, L0_ffn_B, L0_ffn_expert_map)
    return x

_drawn_inputs = setup_inputs


def setup_inputs(seed=0):
    import zlib

    import numpy as np

    out = dict(_drawn_inputs(seed))
    spreads = {}
    factors = {'L0_ffn_base_b': 7.376, 'L0_ffn_router_b': 4.883}
    for name, (base, spread) in spreads.items():
        noise = np.random.default_rng([zlib.crc32(name.encode()), seed]).standard_normal(out[name].shape)
        drawn = base * np.exp(spread * noise) if base else spread * noise
        out[name] = jnp.asarray(drawn.astype(out[name].dtype))
    for name, factor in factors.items():
        out[name] = (out[name] * factor).astype(out[name].dtype)
    return out
```

```python
from contextlib import ExitStack

import concourse.bass as bass
from concourse import mybir

F32 = mybir.dt.float32
F32R = mybir.dt.float32r
I32 = mybir.dt.int32
ALU = mybir.AluOpType
ACT = mybir.ActivationFunctionType
AX = mybir.AxisListType

P = 128
W_SLOTS = 4
C_SLOTS = 3
LORA_SCALE = 32.0 / 16.0


def adaln_ffn_kernel(nc, xT, x, ids, wT, a_t, base_t, b_t, router_t, base_b, router_b, expert_map, out):
    NB, _, KC, T = xT.shape
    OC = wT.shape[1]
    D = KC * P
    NT = T // P
    H = D // 512
    ER = b_t.shape[0]
    NR = expert_map.shape[0]
    E = (NR + 1) // 2
    R = ER // E
    AR = ER + NR + 1
    CHUNK = KC * P
    N_SHARED = 2 + base_t.shape[0]
    TOTAL = NB * OC
    PIECES = 4
    KP = KC // PIECES

    with ExitStack() as ctx:
        def sb(name, shape, dt=F32):
            return ctx.enter_context(nc.sbuf_tensor(name, shape, dt))

        def sem(name):
            return ctx.enter_context(nc.semaphore(name))

        w_raw = sb("w_raw", [P, W_SLOTS, KC, P])
        w_hi = sb("w_hi", [P, W_SLOTS, KC, P], F32R)
        w_lo = sb("w_lo", [P, W_SLOTS, KC, P], F32R)
        x_raw = sb("x_raw", [P, KC, T])
        x_split = sb("x_split", [P, KC, 2, T], F32R)
        y_part = sb("y_part", [P, 2, T])
        y_sum = sb("y_sum", [P, 2, T])
        y_hi = sb("y_hi", [P, KC, T], F32R)
        y_lo = sb("y_lo", [P, KC, T], F32R)
        c_raw = sb("c_raw", [P, C_SLOTS, CHUNK])
        router_raw = sb("router_raw", [P, KC, NR])
        ar_split = sb("ar_split", [P, KC, 2, AR], F32R)
        base_hi = sb("base_hi", [P, H, KC, 512], F32R)
        base_lo = sb("base_lo", [P, H, KC, 512], F32R)
        b_hi = sb("b_hi", [P, D], F32R)
        b_lo = sb("b_lo", [P, D], F32R)
        bias = sb("bias", [P, D])
        router_bias = sb("router_bias", [P, NR])
        map_i = sb("map_i", [P, NR], I32)
        map_f = sb("map_f", [P, NR])
        expert_mask = sb("expert_mask", [P, E, NR])
        ident = sb("ident", [P, P])
        ids_sb = sb("ids_sb", [1, NB], I32)
        res = sb("res", [P, NT, D])
        logits = sb("logits", [P, NT, NR])
        row_max = sb("row_max", [P, NT])
        prob = sb("prob", [P, NT, NR])
        row_sum = sb("row_sum", [P, NT])
        inv_sum = sb("inv_sum", [P, NT])
        top8 = sb("top8", [P, NT, 8])
        marked = sb("marked", [P, NT, NR])
        picked = sb("picked", [P, NT, NR])
        by_expert = sb("by_expert", [P, NT, E, NR])
        gate = sb("gate", [P, NT, E])
        gate_n = sb("gate_n", [P, NT, E])
        h_sum = sb("h_sum", [P, NT, ER])
        hw = sb("hw", [P, NT, ER])
        hwt_hi = sb("hwt_hi", [P, NT, P], F32R)
        hwt_lo = sb("hwt_lo", [P, NT, P], F32R)

        y_ps = ctx.enter_context(nc.psum_tensor("y_ps", [P, 2, 512], F32))
        ar_ps = ctx.enter_context(nc.psum_tensor("ar_ps", [P, NT, 512], F32))
        o_ps = ctx.enter_context(nc.psum_tensor("o_ps", [P, NT, H, 512], F32))
        HWT = 2 * AR

        ids_in = sem("ids_in")
        x0_in = [sem(f"x0_in{j}") for j in range(PIECES)]
        w0_in = [sem(f"w0_in{j}") for j in range(PIECES)]
        x_in = sem("x_in")
        w_in = [sem(f"w_in{s}") for s in range(W_SLOTS)]
        c_in = [sem(f"c_in{s}") for s in range(C_SLOTS)]
        router_in = sem("router_in")
        small_in = sem("small_in")
        res_in = [sem(f"res_in{t}") for t in range(NT)]
        stored = [sem(f"stored{t}") for t in range(NT)]
        x0_hi_done = sem("x0_hi_done")
        x0_lo_done = sem("x0_lo_done")
        w0_hi_done = sem("w0_hi_done")
        w0_lo_done = sem("w0_lo_done")
        x_hi_done = sem("x_hi_done")
        x_lo_done = sem("x_lo_done")
        w_hi_done = sem("w_hi_done")
        w_lo_done = sem("w_lo_done")
        c_hi_done = sem("c_hi_done")
        c_lo_done = sem("c_lo_done")
        router_hi_done = sem("router_hi_done")
        router_lo_done = sem("router_lo_done")
        pad_done = sem("pad_done")
        ident_done = sem("ident_done")
        y_ps_done = sem("y_ps_done")
        y_part_done = sem("y_part_done")
        y_sum_done = sem("y_sum_done")
        y_hi_done = sem("y_hi_done")
        y_lo_done = sem("y_lo_done")
        y_free = sem("y_free")
        ar_done = sem("ar_done")
        shifted = sem("shifted")
        exp_done = sem("exp_done")
        hw_done = sem("hw_done")
        hwt_done = sem("hwt_done")
        hwt_hi_done = sem("hwt_hi_done")
        hwt_lo_done = sem("hwt_lo_done")
        o_ps_done = sem("o_ps_done")
        out_done = sem("out_done")
        res_biased = sem("res_biased")
        chain_done = sem("chain_done")
        gate_done = sem("gate_done")
        mask_done = sem("mask_done")

        block = ctx.enter_context(nc.Block())

        SHARED_AT = {o: o - 2 for o in range(2, OC)}
        SHARED_BEFORE = len(SHARED_AT)
        SHARED_MID = SHARED_BEFORE + 1

        def w_uses(m, slot):
            return m if slot == 0 else m + 1

        def shared_dst(c, part):
            if c == 0:
                return ar_split[:, :, part, 0:ER], c_raw[:, c % C_SLOTS, :].rearrange("p (k e) -> p k e", k=KC)
            if c == N_SHARED - 1:
                return (b_lo if part else b_hi)[:, :], c_raw[:, c % C_SLOTS, :]
            dst = (base_lo if part else base_hi)[:, (c - 1) // (KC // 2), 2 * ((c - 1) % (KC // 2)):2 * ((c - 1) % (KC // 2)) + 2, :]
            return dst, c_raw[:, c % C_SLOTS, :].rearrange("p (k o) -> p k o", k=2)

        @block.sync
        def _(sp):
            sp.dma_start(ids_sb[:, :], ids).then_inc(ids_in, 16)

            def adapter(b):
                return sp.value_load(ids_sb[0:1, bass.ds(b, 1)], min_val=0, max_val=wT.shape[0] - 1)

            def load_x0(j):
                k = slice(j * KP, (j + 1) * KP)
                sp.dma_start(x_raw[:, k, :], xT[0, :, k, :]).then_inc(x0_in[j], 16)

            def load_w(a, o, slot):
                sp.dma_start(w_raw[:, slot, :, :], wT[bass.ds(a, 1), o].rearrange("a p k o -> (a p) k o")).then_inc(w_in[slot], 16)

            def load_shared(c):
                if c >= C_SLOTS:
                    sp.wait_ge(c_lo_done, c - C_SLOTS + 1)
                src = a_t if c == 0 else b_t if c == N_SHARED - 1 else base_t[c - 1]
                sp.dma_start(c_raw[:, c % C_SLOTS, :], src).then_inc(c_in[c % C_SLOTS], 16)

            def load_res(b, t, first):
                if not first:
                    sp.wait_ge(stored[t], 16 * b)
                sp.dma_start(res[:, t, :], x[b, t * P:(t + 1) * P, :] if first else
                             x[bass.ds(b, 1), t * P:(t + 1) * P, :].rearrange("b p d -> (b p) d")).then_inc(res_in[t], 16)

            def store(b, t, halves):
                for h0, n in halves:
                    sp.wait_ge(out_done, NT * H * b + H * t + h0 + n)
                    cols = slice(h0 * 512, (h0 + n) * 512)
                    dst = out[b, t * P:(t + 1) * P, cols] if isinstance(b, int) else \
                        out[bass.ds(b, 1), t * P:(t + 1) * P, cols].rearrange("b p d -> (b p) d")
                    sp.dma_start(dst, res[:, t, cols]).then_inc(stored[t], 16)

            def element(b, first=False, last=False):
                if not last:
                    if first:
                        sp.wait_ge(x0_lo_done, PIECES)
                    else:
                        sp.wait_ge(x_lo_done, 2 * b)
                    sp.dma_start(x_raw[:, :, :], xT[bass.ds(b + 1, 1)].rearrange("b p k t -> (b p) k t")).then_inc(x_in, 16)
                this = adapter(b)
                nxt = None if last else adapter(b + 1)
                for o in range(OC):
                    if o == 0 or not last:
                        sp.wait_ge(w_lo_done, OC * b + 3 + o)
                        load_w(this if o == 0 else nxt, (OC - 1 + o) % OC, (OC - 1 + o) % W_SLOTS)
                    if o in (2, 3) and NT == 2:
                        load_res(b, o - 2, first)
                    if first and C_SLOTS + o < N_SHARED:
                        load_shared(C_SLOTS + o)
                for t in range(NT):
                    store(b, t, [(h, 1) for h in range(H)] if last else [(0, H)])

            load_x0(0)
            sp.wait_ge(ids_in, 16)
            first_id = adapter(0)
            for j in range(PIECES):
                k = slice(j * KP, (j + 1) * KP)
                sp.dma_start(w_raw[:, 0, k, :], wT[bass.ds(first_id, 1), 0, :, k, :].rearrange("a p k o -> (a p) k o")).then_inc(w0_in[j], 16)
                if j + 1 < PIECES:
                    load_x0(j + 1)
            for o in range(1, W_SLOTS):
                load_w(first_id, o, o)
            sp.dma_start(router_raw[:, :, :], router_t).then_inc(router_in, 16)
            load_shared(0)
            for src, dst in ((expert_map, map_i), (router_b, router_bias), (base_b, bias)):
                sp.dma_start(dst[:, :], src.rearrange("(a n) -> a n", a=1).to_broadcast([P, src.shape[0]])).then_inc(small_in, 16)
            for o in range(W_SLOTS, OC - 1):
                if o == W_SLOTS:
                    sp.wait_ge(w0_lo_done, PIECES)
                else:
                    sp.wait_ge(w_lo_done, o - W_SLOTS)
                load_w(first_id, o, o % W_SLOTS)
                if o - W_SLOTS + 1 < C_SLOTS:
                    load_shared(o - W_SLOTS + 1)
            element(0, first=True)
            with sp.Fori(1, NB - 1) as b:
                element(b)
            element(NB - 1, last=True)
            for t in range(NT):
                sp.wait_ge(stored[t], 16 * (NB - 1 + H))

        @block.scalar
        def _(act):
            def shared_hi(c):
                act.wait_ge(c_in[c % C_SLOTS], 16 * (c // C_SLOTS + 1))
                dst, raw = shared_dst(c, 0)
                nc.scalar.copy(dst, raw).then_inc(c_hi_done, 1)

            def adapter_hi(b, o, reused=True):
                slot = o % W_SLOTS
                act.wait_ge(w_in[slot], 16 * w_uses((OC // W_SLOTS) * b + o // W_SLOTS, slot))
                if reused:
                    act.wait_ge(y_ps_done, OC * b + o - W_SLOTS + 1)
                nc.scalar.copy(w_hi[:, slot, :, :], w_raw[:, slot, :, :]).then_inc(w_hi_done, 1)

            def make_y_hi(b, o, first):
                act.wait_ge(y_sum_done, OC * b + o + 1)
                if o == 0 and not first:
                    act.wait_ge(y_free, b)
                nc.scalar.copy(y_hi[:, o, :], y_sum[:, o % 2, :]).then_inc(y_hi_done, 1)

            def element(b, first=False, last=False):
                for o in range(OC):
                    act.wait_ge(y_ps_done, OC * b + o + 1)
                    if not first or o >= 2:
                        act.wait_ge(y_sum_done, OC * b + o - 1)
                    nc.scalar.copy(y_part[:, o % 2, :], y_ps[:, o % 2, T:2 * T]).then_inc(y_part_done, 1)
                    more = not last or o + W_SLOTS < OC
                    if more and o < OC - 1:
                        adapter_hi(b, o + W_SLOTS)
                    make_y_hi(b, o, first)
                    if more and o == OC - 1:
                        adapter_hi(b, o + W_SLOTS)
                    if first and o in SHARED_AT:
                        shared_hi(SHARED_AT[o])
                if not last:
                    act.wait_ge(x_in, 16 * (b + 1))
                    for g in range(2):
                        k = slice(g * KC // 2, (g + 1) * KC // 2)
                        nc.scalar.copy(x_split[:, k, 0, :], x_raw[:, k, :]).then_inc(x_hi_done, 1)
                if first:
                    for c in range(SHARED_BEFORE, SHARED_MID):
                        shared_hi(c)
                act.wait_ge(shifted, b + 1)
                nc.scalar.activation(prob[:, :, :], logits[:, :, :], ACT.Exp).then_inc(exp_done, 1)
                if first:
                    for c in range(SHARED_MID, N_SHARED):
                        shared_hi(c)
                act.wait_ge(hwt_done, b + 1)
                nc.scalar.copy(hwt_hi[:, :, :], ar_ps[:, :, HWT:HWT + P]).then_inc(hwt_hi_done, 1)

            for j in range(PIECES):
                k = slice(j * KP, (j + 1) * KP)
                act.wait_ge(x0_in[j], 16)
                nc.scalar.copy(x_split[:, k, 0, :], x_raw[:, k, :]).then_inc(x0_hi_done, 1)
                act.wait_ge(w0_in[j], 16)
                nc.scalar.copy(w_hi[:, 0, k, :], w_raw[:, 0, k, :]).then_inc(w0_hi_done, 1)
            for o in range(1, W_SLOTS):
                adapter_hi(0, o, reused=False)
            act.wait_ge(router_in, 16)
            nc.scalar.copy(ar_split[:, :, 0, ER:ER + NR], router_raw[:, :, :]).then_inc(router_hi_done, 1)
            element(0, first=True)
            with act.Fori(1, NB - 1) as b:
                element(b)
            element(NB - 1, last=True)

        @block.vector
        def _(dve):
            def shared_lo(c):
                dve.wait_ge(c_hi_done, c + 1)
                hi, raw = shared_dst(c, 0)
                lo, _ = shared_dst(c, 1)
                nc.vector.tensor_tensor(lo, raw, hi, ALU.subtract).then_inc(c_lo_done, 1)

            def adapter_lo(b, o):
                slot = o % W_SLOTS
                dve.wait_ge(w_hi_done, OC * b + o)
                nc.vector.tensor_tensor(w_lo[:, slot, :, :], w_raw[:, slot, :, :], w_hi[:, slot, :, :],
                                        ALU.subtract).then_inc(w_lo_done, 1)

            def x_lo(b, g):
                k = slice(g * KC // 2, (g + 1) * KC // 2)
                dve.wait_ge(x_hi_done, 2 * b + g + 1)
                nc.vector.tensor_tensor(x_split[:, k, 1, :], x_raw[:, k, :], x_split[:, k, 0, :],
                                        ALU.subtract).then_inc(x_lo_done, 1)

            def make_y_lo(b, o):
                dve.wait_ge(y_hi_done, OC * b + o + 1)
                nc.vector.tensor_tensor(y_lo[:, o, :], y_sum[:, o % 2, :], y_hi[:, o, :],
                                        ALU.subtract).then_inc(y_lo_done, 1)

            def per_tile(ap, n):
                return ap.rearrange("p (t n) -> p t n", t=1).to_broadcast([P, NT, n])

            def routing(b):
                at = 13 * b

                def router_part(part):
                    return ar_ps[:, :, part * AR + ER:part * AR + ER + NR]

                dve.wait_ge(ar_done, b + 1)
                nc.vector.tensor_tensor(logits[:, :, :], router_part(0), per_tile(router_bias[:, :], NR),
                                        ALU.add).then_inc(chain_done, 1)
                nc.vector.tensor_copy(h_sum[:, :, :], ar_ps[:, :, 0:ER]).then_inc(chain_done, 1)
                dve.wait_ge(chain_done, at + 1)
                nc.vector.tensor_tensor(logits[:, :, :], logits[:, :, :], router_part(1), ALU.add).then_inc(chain_done, 1)
                dve.wait_ge(chain_done, at + 3)
                nc.vector.tensor_reduce(row_max[:, :], logits[:, :, :], AX.X, ALU.max).then_inc(chain_done, 1)
                dve.wait_ge(chain_done, at + 4)
                nc.vector.tensor_tensor(logits[:, :, :], logits[:, :, :],
                                        row_max[:, :].rearrange("p (t n) -> p t n", n=1).to_broadcast([P, NT, NR]),
                                        ALU.subtract).then_inc(shifted, 1)
                dve.wait_ge(shifted, b + 1)
                nc.vector.tensor_tensor(h_sum[:, :, :], h_sum[:, :, :], ar_ps[:, :, AR:AR + ER],
                                        ALU.add).then_inc(chain_done, 1)
                for t in range(NT):
                    nc.vector.max(top8[:, t, :], logits[:, t, :]).then_inc(chain_done, 1)
                dve.wait_ge(exp_done, b + 1)
                dve.wait_ge(chain_done, at + 7)
                nc.vector.tensor_reduce(row_sum[:, :], prob[:, :, :], AX.X, ALU.add).then_inc(chain_done, 1)
                for t in range(NT):
                    nc.vector.match_replace(marked[:, t, :], top8[:, t, :], logits[:, t, :], 1.0).then_inc(chain_done, 1)
                dve.wait_ge(chain_done, at + 10)
                nc.vector.scalar_tensor_tensor(out=picked[:, :, :], in0=marked[:, :, :], scalar=0.0,
                                               in1=prob[:, :, :], op0=ALU.is_gt, op1=ALU.mult).then_inc(chain_done, 1)
                dve.wait_ge(chain_done, at + 11)
                nc.vector.tensor_tensor(by_expert[:, :, :, :],
                                        picked[:, :, :].rearrange("p t (e n) -> p t e n", e=1).to_broadcast([P, NT, E, NR]),
                                        expert_mask[:, :, :].rearrange("p (t e) n -> p t e n", t=1).to_broadcast([P, NT, E, NR]),
                                        ALU.mult).then_inc(chain_done, 1)
                nc.vector.reciprocal(inv_sum[:, :], row_sum[:, :]).then_inc(chain_done, 1)
                dve.wait_ge(chain_done, at + 12)
                nc.vector.tensor_reduce(gate[:, :, :], by_expert[:, :, :, :], AX.X, ALU.add).then_inc(gate_done, 1)
                dve.wait_ge(gate_done, 2 * b + 1)
                nc.vector.scalar_tensor_tensor(out=gate_n[:, :, :], in0=gate[:, :, :], scalar=LORA_SCALE,
                                               in1=inv_sum[:, :].rearrange("p (t n) -> p t n", n=1).to_broadcast([P, NT, E]),
                                               op0=ALU.mult, op1=ALU.mult).then_inc(gate_done, 1)
                dve.wait_ge(gate_done, 2 * b + 2)
                nc.vector.tensor_tensor(hw[:, :, :].rearrange("p t (e r) -> p t e r", e=E),
                                        h_sum[:, :, :].rearrange("p t (e r) -> p t e r", e=E),
                                        gate_n[:, :, :].rearrange("p t (e r) -> p t e r", r=1).to_broadcast([P, NT, E, R]),
                                        ALU.mult).then_inc(hw_done, 1)

            def element(b, first=False, last=False):
                for o in range(OC):
                    dve.wait_ge(y_part_done, OC * b + o + 1)
                    nc.vector.tensor_tensor(y_sum[:, o % 2, :], y_ps[:, o % 2, 0:T], y_part[:, o % 2, :],
                                            ALU.add).then_inc(y_sum_done, 1)
                    more = not last or o + W_SLOTS - 1 < OC
                    if more and o < OC - 1:
                        adapter_lo(b, o + W_SLOTS - 1)
                    make_y_lo(b, o)
                    if more and o == OC - 1:
                        adapter_lo(b, o + W_SLOTS - 1)
                    if first and o in SHARED_AT:
                        shared_lo(SHARED_AT[o])
                if not last:
                    x_lo(b, 0)
                if first:
                    for c in range(SHARED_BEFORE, SHARED_MID):
                        shared_lo(c)
                routing(b)
                if first:
                    for c in range(SHARED_MID, N_SHARED):
                        shared_lo(c)
                if not last:
                    x_lo(b, 1)
                dve.wait_ge(hwt_hi_done, b + 1)
                nc.vector.tensor_tensor(hwt_lo[:, :, :], ar_ps[:, :, HWT:HWT + P], hwt_hi[:, :, :],
                                        ALU.subtract).then_inc(hwt_lo_done, 1)
                for t in range(NT):
                    dve.wait_ge(res_in[t], 16 * (b + 1))
                    nc.vector.tensor_tensor(res[:, t, :], res[:, t, :], bias[:, :], ALU.add).then_inc(res_biased, 1)
                for t in range(NT):
                    dve.wait_ge(res_biased, NT * b + t + 1)
                    for h in range(H):
                        dve.wait_ge(o_ps_done, NT * H * b + H * t + h + 1)
                        cols = slice(h * 512, (h + 1) * 512)
                        nc.vector.tensor_tensor(res[:, t, cols], o_ps[:, t, h, :], res[:, t, cols],
                                                ALU.add).then_inc(out_done, 1)

            for j in range(PIECES):
                k = slice(j * KP, (j + 1) * KP)
                dve.wait_ge(x0_hi_done, j + 1)
                nc.vector.tensor_tensor(x_split[:, k, 1, :], x_raw[:, k, :], x_split[:, k, 0, :],
                                        ALU.subtract).then_inc(x0_lo_done, 1)
                dve.wait_ge(w0_hi_done, j + 1)
                nc.vector.tensor_tensor(w_lo[:, 0, k, :], w_raw[:, 0, k, :], w_hi[:, 0, k, :],
                                        ALU.subtract).then_inc(w0_lo_done, 1)
            for o in range(1, W_SLOTS - 1):
                adapter_lo(0, o)
            dve.wait_ge(router_hi_done, 1)
            nc.vector.tensor_tensor(ar_split[:, :, 1, ER:ER + NR], router_raw[:, :, :], ar_split[:, :, 0, ER:ER + NR],
                                    ALU.subtract).then_inc(router_lo_done, 1)
            dve.wait_ge(small_in, 48)
            nc.vector.tensor_copy(map_f[:, :], map_i[:, :]).then_inc(mask_done, 1)
            dve.wait_ge(mask_done, 1)
            for e in range(E):
                nc.vector.tensor_scalar(expert_mask[:, e, :], map_f[:, :], float(e), None, ALU.is_equal).then_inc(mask_done, 1)
            dve.wait_ge(mask_done, 1 + E)
            element(0, first=True)
            with dve.Fori(1, NB - 1) as b:
                element(b)
            element(NB - 1, last=True)

        @block.tensor
        def _(pe):
            def stage1(b, first):
                for o in range(OC):
                    slot = o % W_SLOTS
                    if not first or o > 0:
                        pe.wait_ge(w_lo_done, OC * b + o)
                    if not first and o == 0:
                        pe.wait_ge(x_lo_done, 2 * b)
                    if not first or o >= 2:
                        pe.wait_ge(y_sum_done, OC * b + o - 1)
                    for k in range(KC):
                        if first and o == 0 and k % KP == 0:
                            pe.wait_ge(w0_lo_done, k // KP + 1)
                        nc.tensor.matmul(y_ps[:, o % 2, :], w_hi[:, slot, k, :],
                                         x_split[:, k, :, :].rearrange("p s t -> p (s t)"), start=(k == 0), stop=False)
                        mm = nc.tensor.matmul(y_ps[:, o % 2, 0:T], w_lo[:, slot, k, :], x_split[:, k, 0, :],
                                              start=False, stop=(k == KC - 1))
                    mm.then_inc(y_ps_done, 1)

            def lora_a(b, t, ks):
                for k in ks:
                    mm = tile_matmul(ar_ps[:, t, 0:2 * AR], y_hi, t, k, ar_split[:, k, :, :].rearrange("p s n -> p (s n)"), k == 0, False)
                    mm = tile_matmul(ar_ps[:, t, 0:AR], y_lo, t, k, ar_split[:, k, 0, :], False, k == KC - 1)
                return mm

            def tile_matmul(dst, y, t, k, moving, start, stop):
                return nc.tensor.matmul(dst, y[:, k, t * P:(t + 1) * P], moving, start=start, stop=stop)

            def base(b, t, h, first):
                if not first:
                    pe.wait_ge(out_done, NT * H * (b - 1) + H * t + h + 1)
                for k in range(KC):
                    if first and t == 0 and k % 2 == 0:
                        pe.wait_ge(c_lo_done, 2 + h * (KC // 2) + k // 2)
                    tile_matmul(o_ps[:, t, h, :], y_hi, t, k, base_hi[:, h, k, :], k == 0, False)
                    tile_matmul(o_ps[:, t, h, :], y_hi, t, k, base_lo[:, h, k, :], False, False)
                    mm = tile_matmul(o_ps[:, t, h, :], y_lo, t, k, base_hi[:, h, k, :], False, False)
                return mm

            def lora_b(t, h):
                cols = slice(h * 512, (h + 1) * 512)
                nc.tensor.matmul(o_ps[:, t, h, :], hwt_hi[:, t, :], b_hi[:, cols], start=False, stop=False)
                nc.tensor.matmul(o_ps[:, t, h, :], hwt_hi[:, t, :], b_lo[:, cols], start=False, stop=False)
                nc.tensor.matmul(o_ps[:, t, h, :], hwt_lo[:, t, :], b_hi[:, cols], start=False, stop=True).then_inc(o_ps_done, 1)

            def stage2(b, first):
                if first:
                    pe.wait_ge(c_lo_done, 1)
                    pe.wait_ge(router_lo_done, 1)
                    pe.wait_ge(pad_done, 1)
                else:
                    pe.wait_ge(hwt_lo_done, b)
                pe.wait_ge(y_lo_done, OC * (b + 1) - 1)
                for t in range(NT):
                    lora_a(b, t, range(KC - 1))
                pe.wait_ge(y_lo_done, OC * (b + 1))
                for t in range(NT):
                    mm = lora_a(b, t, range(KC - 1, KC))
                mm.then_inc(ar_done, 1)
                base(b, 0, 0, first)
                if first:
                    base(b, 0, 1, first)
                pe.wait_ge(hw_done, b + 1)
                if first:
                    pe.wait_ge(ident_done, 2)
                for t in range(NT):
                    mm = nc.tensor.transpose(ar_ps[:, t, HWT:HWT + P], hw[:, t, :], ident[:, :])
                mm.then_inc(hwt_done, 1)
                base(b, 1 if first else 0, 0 if first else 1, first)
                if first:
                    pe.wait_ge(c_lo_done, N_SHARED)
                pe.wait_ge(hwt_lo_done, b + 1)
                lora_b(0, 0)
                lora_b(0, 1)
                if not first:
                    base(b, 1, 0, first)
                lora_b(1, 0)
                base(b, 1, 1, first).then_inc(y_free, 1)
                lora_b(1, 1)

            stage1(0, True)
            stage2(0, True)
            with pe.Fori(1, NB - 1) as b:
                stage1(b, False)
                stage2(b, False)
            stage1(NB - 1, False)
            stage2(NB - 1, False)

        @block.gpsimd
        def _(pool):
            nc.gpsimd.memset(ar_split[:, :, :, AR - 1:AR].bitcast(F32), 0.0).then_inc(pad_done, 1)
            nc.gpsimd.memset(ident[:, :], 0.0).then_inc(ident_done, 1)
            pool.wait_ge(ident_done, 1)
            nc.gpsimd.affine_select(out=ident[:, :], in_=ident[:, :], compare_op=ALU.not_equal, fill=1.0, base=0,
                                    pattern=[[-1, P]], channel_multiplier=1).then_inc(ident_done, 1)


def kernel(x, itok_B_3_7, L0_cond_weight, L0_ffn_base_W, L0_ffn_base_b, L0_ffn_router_W, L0_ffn_router_b,
           L0_ffn_A, L0_ffn_B, L0_ffn_expert_map):
    import numpy as np
    import concourse.bacc as bacc
    from concourse.bass_utils import run_bass_kernel_spmd

    nc = bacc.Bacc("TRN2", target_bir_lowering=False, num_devices=1)
    NB, T, D = x.shape
    NA = L0_cond_weight.shape[0]
    E, R, _ = L0_ffn_A.shape
    NR = L0_ffn_router_W.shape[0]
    KC = D // P
    x, cond, base, a, bm, router = (np.asarray(v) for v in (x, L0_cond_weight, L0_ffn_base_W, L0_ffn_A, L0_ffn_B, L0_ffn_router_W))
    arrays = {
        "xT": x.reshape(NB, T, KC, P).transpose(0, 3, 2, 1),
        "x": x,
        "ids": np.asarray(itok_B_3_7).reshape(1, NB),
        "wT": cond.reshape(NA, KC, P, KC, P).transpose(0, 1, 4, 3, 2),
        "a_t": a.reshape(E * R, KC, P).transpose(2, 1, 0).reshape(P, KC * E * R),
        "base_t": base.reshape(D // 512, 512, KC // 2, 2, P).transpose(0, 2, 4, 3, 1).reshape(D // 512 * KC // 2, P, 2 * 512),
        "b_t": bm.transpose(0, 2, 1).reshape(E * R, D),
        "router_t": router.reshape(NR, KC, P).transpose(2, 1, 0),
        "base_b": np.asarray(L0_ffn_base_b),
        "router_b": np.asarray(L0_ffn_router_b),
        "expert_map": np.asarray(L0_ffn_expert_map),
    }
    arrays = {name: np.ascontiguousarray(v) for name, v in arrays.items()}
    args = [nc.dram_tensor(f"in_{name}", v.shape, mybir.dt.from_np(v.dtype), kind="ExternalInput").ap() for name, v in arrays.items()]
    args.append(nc.dram_tensor("out", (NB, T, D), F32, kind="ExternalOutput").ap())
    adaln_ffn_kernel(nc, *args)
    result = run_bass_kernel_spmd(nc, [{f"in_{name}": v for name, v in arrays.items()}], core_ids=[0])
    return result.results[0]["out"]
```

```python
from contextlib import ExitStack

import concourse.bass as bass
from concourse import mybir

F32 = mybir.dt.float32
F32R = mybir.dt.float32r
I32 = mybir.dt.int32
ALU = mybir.AluOpType
ACT = mybir.ActivationFunctionType
AX = mybir.AxisListType

P = 128
W_SLOTS = 4
F32_CHUNKS = 2
C_SLOTS = 4
LORA_SCALE = 32.0 / 16.0
WARM_UP = 10
MARK = 3.0e38


def adaln_ffn_kernel(nc, xT, x, ids, wT, a_t, base_t, b_t, router_t, base_b, router_b, expert_map, out):
    NB, _, KC, T = xT.shape
    OC = wT.shape[1]
    D = KC * P
    NT = T // P
    ER = b_t.shape[0]
    NR = expert_map.shape[0]
    E = (NR + 1) // 2
    R = ER // E
    AR = ER + NR + 1
    NG = 3
    GROUP = (AR + D) // NG // 8 * 8 + 8
    EDGE = [0, AR + D - 2 * GROUP, AR + D - GROUP, AR + D]
    HWT = EDGE[1]
    assert EDGE[1] + P <= 512 and GROUP <= 512 and EDGE[1] > AR
    OUT = [0] + [e - AR for e in EDGE[1:]]
    CHUNK = KC * P
    PARTS = [(g, range(j, j + n)) for g, n in ((0, KC // 2), (1, 2), (2, 2)) for j in range(0, KC, n)]
    N_SHARED = 2 + len(PARTS)
    PIECES = 4
    KP = KC // PIECES

    with ExitStack() as ctx:
        def sb(name, shape, dt=F32):
            return ctx.enter_context(nc.sbuf_tensor(name, shape, dt))

        def sem(name):
            return ctx.enter_context(nc.semaphore(name))

        w_raw = sb("w_raw", [P, W_SLOTS, KC, P])
        w_hi = sb("w_hi", [P, W_SLOTS, KC, P], F32R)
        w_lo = sb("w_lo", [P, W_SLOTS, KC, P], F32R)
        x_raw = sb("x_raw", [P, KC, T])
        x_split = sb("x_split", [P, KC, 2, T], F32R)
        y_part = sb("y_part", [P, 2, T])
        y_sum = sb("y_sum", [P, 2, T])
        y_hi = sb("y_hi", [P, KC, T], F32R)
        y_lo = sb("y_lo", [P, KC, T], F32R)
        c_raw = sb("c_raw", [P, C_SLOTS, CHUNK])
        router_raw = sb("router_raw", [P, KC, NR])
        s2_hi = sb("s2_hi", [P, KC, AR + D], F32R)
        s2_lo = sb("s2_lo", [P, KC, AR + D], F32R)
        b_hi = sb("b_hi", [P, D], F32R)
        b_lo = sb("b_lo", [P, D], F32R)
        bias = sb("bias", [P, D])
        router_bias = sb("router_bias", [P, NR])
        map_i = sb("map_i", [P, NR], I32)
        map_f = sb("map_f", [P, NR])
        expert_mask = sb("expert_mask", [P, E, NR])
        ident = sb("ident", [P, P])
        ids_sb = sb("ids_sb", [1, NB], I32)
        res = sb("res", [P, NT, D])
        logits = sb("logits", [P, NT, NR])
        shift = sb("shift", [P, NT, NR])
        row_max = sb("row_max", [P, NT])
        prob = sb("prob", [P, NT, NR])
        row_sum = sb("row_sum", [P, NT])
        inv_sum = sb("inv_sum", [P, NT])
        top8 = sb("top8", [P, NT, 8])
        marked = sb("marked", [P, NT, NR])
        picked = sb("picked", [P, NT, NR])
        by_expert = sb("by_expert", [P, NT, E, NR])
        gate = sb("gate", [P, NT, E])
        gate_n = sb("gate_n", [P, NT, E])
        hw = sb("hw", [P, NT, ER])
        hwt_hi = sb("hwt_hi", [P, NT, P], F32R)
        hwt_lo = sb("hwt_lo", [P, NT, P], F32R)

        y_ps = ctx.enter_context(nc.psum_tensor("y_ps", [P, 2, 512], F32))
        s2_ps = ctx.enter_context(nc.psum_tensor("s2_ps", [P, NG, NT, 512], F32))

        ids_in = sem("ids_in")
        x0_in = [sem(f"x0_in{j}") for j in range(PIECES)]
        w0_in = [sem(f"w0_in{j}") for j in range(PIECES)]
        x_in = sem("x_in")
        w_in = [sem(f"w_in{s}") for s in range(W_SLOTS)]
        c_in = [sem(f"c_in{s}") for s in range(C_SLOTS)]
        router_in = sem("router_in")
        small_in = sem("small_in")
        res_in = [sem(f"res_in{t}") for t in range(NT)]
        stored = [sem(f"stored{t}") for t in range(NT)]
        x0_hi_done = sem("x0_hi_done")
        x0_lo_done = sem("x0_lo_done")
        x_hi_done = sem("x_hi_done")
        x_lo_done = sem("x_lo_done")
        w_hi_done = sem("w_hi_done")
        w_lo_done = sem("w_lo_done")
        c_hi_done = sem("c_hi_done")
        c_lo_done = sem("c_lo_done")
        router_hi_done = sem("router_hi_done")
        router_lo_done = sem("router_lo_done")
        pad_done = sem("pad_done")
        ident_done = sem("ident_done")
        y_ps_done = sem("y_ps_done")
        y_part_done = sem("y_part_done")
        y_sum_done = sem("y_sum_done")
        y_hi_done = sem("y_hi_done")
        y_lo_done = sem("y_lo_done")
        y_free = sem("y_free")
        ar_done = sem("ar_done")
        shifted = sem("shifted")
        exp_done = sem("exp_done")
        hw_done = sem("hw_done")
        hwt_done = sem("hwt_done")
        hwt_hi_done = sem("hwt_hi_done")
        hwt_lo_done = sem("hwt_lo_done")
        s2_ps_done = sem("s2_ps_done")
        out_done = sem("out_done")
        res_biased = sem("res_biased")
        chain_done = sem("chain_done")
        gate_done = sem("gate_done")
        mask_done = sem("mask_done")

        block = ctx.enter_context(nc.Block())

        SHARED_AT = {o: o - 2 for o in range(2, OC)}

        def w_uses(m, slot):
            return m if slot == 0 else m + 1

        def split(b, o):
            return OC * b + o - F32_CHUNKS + 1

        def shared(c):
            raw = c_raw[:, c % C_SLOTS, :]
            if c == 0:
                return a_t, raw.rearrange("p (k e) -> p k e", k=KC), s2_hi[:, :, 0:ER], s2_lo[:, :, 0:ER]
            if c == N_SHARED - 1:
                return b_t, raw, b_hi[:, :], b_lo[:, :]
            g, ks = PARTS[c - 1]
            n = OUT[g + 1] - OUT[g]
            k = slice(ks.start, ks.stop)
            cols = slice(AR + OUT[g], AR + OUT[g + 1])
            return (base_t[:, k, OUT[g]:OUT[g + 1]], raw[:, 0:len(ks) * n].rearrange("p (k n) -> p k n", n=n),
                    s2_hi[:, k, cols], s2_lo[:, k, cols])

        @block.sync
        def _(sp):
            sp.dma_start(ids_sb[:, :], ids).then_inc(ids_in, 16)

            def adapter(b):
                return sp.value_load(ids_sb[0:1, bass.ds(b, 1)], min_val=0, max_val=wT.shape[0] - 1)

            def load_x0(j):
                k = slice(j * KP, (j + 1) * KP)
                sp.dma_start(x_raw[:, k, :], xT[0, :, k, :]).then_inc(x0_in[j], 16)

            def load_w(a, o, slot):
                sp.dma_start(w_raw[:, slot, :, :], wT[bass.ds(a, 1), o].rearrange("a p k o -> (a p) k o")).then_inc(w_in[slot], 16)

            def load_shared(c):
                if c >= C_SLOTS:
                    sp.wait_ge(c_lo_done, c - C_SLOTS + 1)
                src, raw, _, _ = shared(c)
                sp.dma_start(raw, src).then_inc(c_in[c % C_SLOTS], 16)

            def load_res(b, t, first=False):
                if not first:
                    sp.wait_ge(stored[t], 16 * b)
                sp.dma_start(res[:, t, :], x[b, t * P:(t + 1) * P, :] if first else
                             x[bass.ds(b, 1), t * P:(t + 1) * P, :].rearrange("b p d -> (b p) d")).then_inc(res_in[t], 16)

            def store(b, t, group_runs):
                for g0, g1 in group_runs:
                    sp.wait_ge(out_done, NG * (NT * b + t) + g1)
                    cols = slice(OUT[g0], OUT[g1])
                    dst = out[b, t * P:(t + 1) * P, cols] if isinstance(b, int) else \
                        out[bass.ds(b, 1), t * P:(t + 1) * P, cols].rearrange("b p d -> (b p) d")
                    sp.dma_start(dst, res[:, t, cols]).then_inc(stored[t], 16)

            def element(b, last=False):
                if not last:
                    sp.wait_ge(x_lo_done, 2 * b)
                    sp.dma_start(x_raw[:, :, :], xT[bass.ds(b + 1, 1)].rearrange("b p k t -> (b p) k t")).then_inc(x_in, 16)
                this = adapter(b)
                nxt = None if last else adapter(b + 1)
                for o in range(OC):
                    if o == 0 or not last:
                        sp.wait_ge(w_lo_done, split(b, 3 + o))
                        load_w(this if o == 0 else nxt, (OC - 1 + o) % OC, (OC - 1 + o) % W_SLOTS)
                    if o in (2, 3):
                        load_res(b, o - 2)
                for t in range(NT):
                    store(b, t, [(0, 2), (2, 3)] if last and t == NT - 1 else [(0, NG)])

            load_x0(0)
            load_x0(1)
            sp.wait_ge(ids_in, 16)
            id0 = adapter(0)
            for j in range(PIECES):
                k = slice(j * KP, (j + 1) * KP)
                sp.dma_start(w_raw[:, 0, k, :], wT[bass.ds(id0, 1), 0, :, k, :].rearrange("a p k o -> (a p) k o")).then_inc(w0_in[j], 16)
                if j + 2 < PIECES:
                    load_x0(j + 2)
            for o in range(1, W_SLOTS):
                load_w(id0, o, o)
            for o in range(W_SLOTS, OC):
                if o - W_SLOTS < F32_CHUNKS:
                    sp.wait_ge(y_ps_done, o - W_SLOTS + 1)
                else:
                    sp.wait_ge(w_lo_done, split(0, o - W_SLOTS))
                load_w(id0, o, o % W_SLOTS)
                if o == W_SLOTS:
                    sp.dma_start(router_raw[:, :, :], router_t).then_inc(router_in, 16)
                load_shared(o - W_SLOTS)
            for src, dst in ((expert_map, map_i), (router_b, router_bias), (base_b, bias)):
                sp.dma_start(dst[:, :], src.rearrange("(a n) -> a n", a=1).to_broadcast([P, src.shape[0]])).then_inc(small_in, 16)
            for c in range(OC - W_SLOTS, N_SHARED):
                load_shared(c)
            sp.wait_ge(x0_lo_done, PIECES)
            sp.wait_ge(y_ps_done, F32_CHUNKS)
            sp.dma_start(x_raw[:, :, :], xT[1]).then_inc(x_in, 16)
            id1 = adapter(1)
            for o in range(OC - 1):
                sp.wait_ge(w_lo_done, split(0, OC + o - W_SLOTS))
                load_w(id1, o, o % W_SLOTS)
                if o in (4, 5):
                    load_res(0, o - 4, first=True)
            for t in range(NT):
                store(0, t, [(0, NG)])

            with sp.Fori(1, NB - 1) as b:
                element(b)
            element(NB - 1, last=True)
            for t in range(NT):
                sp.wait_ge(stored[t], 16 * (NB + (t == NT - 1)))

        @block.scalar
        def _(act):
            def shared_hi(c):
                act.wait_ge(c_in[c % C_SLOTS], 16 * (c // C_SLOTS + 1))
                _, raw, hi, _ = shared(c)
                nc.scalar.copy(hi, raw).then_inc(c_hi_done, 1)

            def adapter_hi(b, o, reused=True):
                slot = o % W_SLOTS
                act.wait_ge(w_in[slot], 16 * w_uses((OC // W_SLOTS) * b + o // W_SLOTS, slot))
                if reused:
                    act.wait_ge(y_ps_done, OC * b + o - W_SLOTS + 1)
                nc.scalar.copy(w_hi[:, slot, :, :], w_raw[:, slot, :, :]).then_inc(w_hi_done, 1)

            def make_y_part(b, o, first=False):
                act.wait_ge(y_ps_done, OC * b + o + 1)
                if not first or o >= F32_CHUNKS + 2:
                    act.wait_ge(y_sum_done, OC * b + o - 1)
                nc.scalar.copy(y_part[:, o % 2, :], y_ps[:, o % 2, T:2 * T]).then_inc(y_part_done, 1)

            def make_y_hi(b, o, first=False):
                act.wait_ge(y_sum_done, OC * b + o + 1)
                if o == 0 and not first:
                    act.wait_ge(y_free, b)
                nc.scalar.copy(y_hi[:, o, :], y_sum[:, o % 2, :]).then_inc(y_hi_done, 1)

            def x_hi(b):
                act.wait_ge(x_in, 16 * (b + 1))
                for g in range(2):
                    k = slice(g * KC // 2, (g + 1) * KC // 2)
                    nc.scalar.copy(x_split[:, k, 0, :], x_raw[:, k, :]).then_inc(x_hi_done, 1)

            def exponential(b):
                act.wait_ge(shifted, b + 1)
                nc.scalar.activation(prob[:, :, :], shift[:, :, :], ACT.Exp).then_inc(exp_done, 1)

            def make_hwt_hi(b):
                act.wait_ge(hwt_done, b + 1)
                nc.scalar.copy(hwt_hi[:, :, :], s2_ps[:, 0, :, HWT:HWT + P]).then_inc(hwt_hi_done, 1)

            def element(b, last=False):
                for o in range(OC):
                    make_y_part(b, o)
                    more = not last or o + W_SLOTS < OC
                    if more and o < OC - 1:
                        adapter_hi(b, o + W_SLOTS)
                    make_y_hi(b, o)
                    if more and o == OC - 1:
                        adapter_hi(b, o + W_SLOTS)
                if not last:
                    x_hi(b)
                exponential(b)
                make_hwt_hi(b)

            for j in range(PIECES):
                k = slice(j * KP, (j + 1) * KP)
                act.wait_ge(x0_in[j], 16)
                nc.scalar.copy(x_split[:, k, 0, :], x_raw[:, k, :]).then_inc(x0_hi_done, 1)
            make_y_hi(0, 0, first=True)
            for o in range(F32_CHUNKS, W_SLOTS):
                adapter_hi(0, o, reused=False)
            for o in range(1, OC):
                if o >= F32_CHUNKS:
                    make_y_part(0, o, first=True)
                if o < F32_CHUNKS:
                    make_y_hi(0, o, first=True)
                if o + 3 < OC:
                    adapter_hi(0, o + 3, reused=o + 3 - W_SLOTS >= F32_CHUNKS)
                if o == 1:
                    act.wait_ge(router_in, 16)
                    nc.scalar.copy(s2_hi[:, :, ER:ER + NR], router_raw[:, :, :]).then_inc(router_hi_done, 1)
                if o >= F32_CHUNKS:
                    make_y_hi(0, o, first=True)
                if o in SHARED_AT:
                    shared_hi(SHARED_AT[o])
            for c in range(len(SHARED_AT), N_SHARED - 1):
                shared_hi(c)
            exponential(0)
            shared_hi(N_SHARED - 1)
            x_hi(0)
            make_hwt_hi(0)
            for o in range(OC, OC + W_SLOTS):
                adapter_hi(0, o)

            with act.Fori(1, NB - 1) as b:
                element(b)
            element(NB - 1, last=True)

        @block.vector
        def _(dve):
            def shared_lo(c):
                dve.wait_ge(c_hi_done, c + 1)
                _, raw, hi, lo = shared(c)
                nc.vector.tensor_tensor(lo, raw, hi, ALU.subtract).then_inc(c_lo_done, 1)

            def adapter_lo(b, o):
                slot = o % W_SLOTS
                dve.wait_ge(w_hi_done, split(b, o))
                nc.vector.tensor_tensor(w_lo[:, slot, :, :], w_raw[:, slot, :, :], w_hi[:, slot, :, :],
                                        ALU.subtract).then_inc(w_lo_done, 1)

            def x_lo(b, g):
                k = slice(g * KC // 2, (g + 1) * KC // 2)
                dve.wait_ge(x_hi_done, 2 * b + g + 1)
                nc.vector.tensor_tensor(x_split[:, k, 1, :], x_raw[:, k, :], x_split[:, k, 0, :],
                                        ALU.subtract).then_inc(x_lo_done, 1)

            def make_y_lo(b, o):
                dve.wait_ge(y_hi_done, OC * b + o + 1)
                nc.vector.tensor_tensor(y_lo[:, o, :], y_sum[:, o % 2, :], y_hi[:, o, :],
                                        ALU.subtract).then_inc(y_lo_done, 1)

            def per_tile(ap, n):
                return ap.rearrange("p (t n) -> p t n", t=1).to_broadcast([P, NT, n])

            def routing(b):
                at = 11 * b
                dve.wait_ge(ar_done, b + 1)
                nc.vector.tensor_tensor(logits[:, :, :], s2_ps[:, 0, :, ER:ER + NR], per_tile(router_bias[:, :], NR),
                                        ALU.add).then_inc(chain_done, 1)
                dve.wait_ge(chain_done, at + 1)
                nc.vector.tensor_reduce(row_max[:, :], logits[:, :, :], AX.X, ALU.max).then_inc(chain_done, 1)
                for t in range(NT):
                    nc.vector.max(top8[:, t, :], logits[:, t, :]).then_inc(chain_done, 1)
                dve.wait_ge(chain_done, at + 4)
                nc.vector.tensor_tensor(shift[:, :, :], logits[:, :, :],
                                        row_max[:, :].rearrange("p (t n) -> p t n", n=1).to_broadcast([P, NT, NR]),
                                        ALU.subtract).then_inc(shifted, 1)
                for t in range(NT):
                    nc.vector.match_replace(marked[:, t, :], top8[:, t, :], logits[:, t, :], MARK).then_inc(chain_done, 1)
                dve.wait_ge(exp_done, b + 1)
                nc.vector.tensor_reduce(row_sum[:, :], prob[:, :, :], AX.X, ALU.add).then_inc(chain_done, 1)
                dve.wait_ge(chain_done, at + 6)
                for t in range(NT):
                    nc.vector.scalar_tensor_tensor(out=picked[:, t, :], in0=marked[:, t, :], scalar=row_max[:, t:t + 1],
                                                   in1=prob[:, t, :], op0=ALU.is_gt, op1=ALU.mult).then_inc(chain_done, 1)
                dve.wait_ge(chain_done, at + 9)
                nc.vector.tensor_tensor(by_expert[:, :, :, :],
                                        picked[:, :, :].rearrange("p t (e n) -> p t e n", e=1).to_broadcast([P, NT, E, NR]),
                                        expert_mask[:, :, :].rearrange("p (t e) n -> p t e n", t=1).to_broadcast([P, NT, E, NR]),
                                        ALU.mult).then_inc(chain_done, 1)
                nc.vector.reciprocal(inv_sum[:, :], row_sum[:, :]).then_inc(chain_done, 1)
                dve.wait_ge(chain_done, at + 10)
                nc.vector.tensor_reduce(gate[:, :, :], by_expert[:, :, :, :], AX.X, ALU.add).then_inc(gate_done, 1)
                dve.wait_ge(gate_done, 2 * b + 1)
                nc.vector.scalar_tensor_tensor(out=gate_n[:, :, :], in0=gate[:, :, :], scalar=LORA_SCALE,
                                               in1=inv_sum[:, :].rearrange("p (t n) -> p t n", n=1).to_broadcast([P, NT, E]),
                                               op0=ALU.mult, op1=ALU.mult).then_inc(gate_done, 1)
                dve.wait_ge(gate_done, 2 * b + 2)
                nc.vector.tensor_tensor(hw[:, :, :].rearrange("p t (e r) -> p t e r", e=E),
                                        s2_ps[:, 0, :, 0:ER].rearrange("p t (e r) -> p t e r", e=E),
                                        gate_n[:, :, :].rearrange("p t (e r) -> p t e r", r=1).to_broadcast([P, NT, E, R]),
                                        ALU.mult).then_inc(hw_done, 1)

            def add_bias(b):
                for t in range(NT):
                    dve.wait_ge(res_in[t], 16 * (b + 1))
                    nc.vector.tensor_tensor(res[:, t, :], res[:, t, :], bias[:, :], ALU.add).then_inc(res_biased, 1)

            def make_hwt_lo(b):
                dve.wait_ge(hwt_hi_done, b + 1)
                nc.vector.tensor_tensor(hwt_lo[:, :, :], s2_ps[:, 0, :, HWT:HWT + P], hwt_hi[:, :, :],
                                        ALU.subtract).then_inc(hwt_lo_done, 1)

            def output(b):
                for t in range(NT):
                    dve.wait_ge(res_biased, NT * b + t + 1)
                    for g in range(NG):
                        dve.wait_ge(s2_ps_done, NG * (NT * b + t) + g + 1)
                        cols = slice(OUT[g], OUT[g + 1])
                        skip = AR if g == 0 else 0
                        nc.vector.tensor_tensor(res[:, t, cols], s2_ps[:, g, t, skip:skip + OUT[g + 1] - OUT[g]],
                                                res[:, t, cols], ALU.add).then_inc(out_done, 1)

            def make_y_sum(b, o):
                dve.wait_ge(y_part_done, split(b, o))
                nc.vector.tensor_tensor(y_sum[:, o % 2, :], y_ps[:, o % 2, 0:T], y_part[:, o % 2, :],
                                        ALU.add).then_inc(y_sum_done, 1)

            def element(b, last=False):
                for o in range(OC):
                    make_y_sum(b, o)
                    more = not last or o + W_SLOTS - 1 < OC
                    if more and o < OC - 1:
                        adapter_lo(b, o + W_SLOTS - 1)
                    make_y_lo(b, o)
                    if more and o == OC - 1:
                        adapter_lo(b, o + W_SLOTS - 1)
                if not last:
                    x_lo(b, 0)
                    x_lo(b, 1)
                routing(b)
                add_bias(b)
                make_hwt_lo(b)
                output(b)

            for j in range(PIECES):
                k = slice(j * KP, (j + 1) * KP)
                dve.wait_ge(x0_hi_done, j + 1)
                nc.vector.tensor_tensor(x_split[:, k, 1, :], x_raw[:, k, :], x_split[:, k, 0, :],
                                        ALU.subtract).then_inc(x0_lo_done, 1)
            steps = [("w2", ""), ("w3", ""), ("w4", ""), ("w5", "w6"), ("c0", "w7"), ("c1", "c2"), ("", "c3"), ("", "c4")]

            def split_lo(what):
                if what:
                    n = int(what[1:])
                    adapter_lo(0, n) if what[0] == "w" else shared_lo(n)

            for o, (before, after) in enumerate(steps):
                if o < F32_CHUNKS:
                    dve.wait_ge(y_ps_done, o + 1)
                    nc.vector.tensor_copy(y_sum[:, o, :], y_ps[:, o, 0:T]).then_inc(y_sum_done, 1)
                else:
                    make_y_sum(0, o)
                split_lo(before)
                make_y_lo(0, o)
                split_lo(after)
                if o == 2:
                    dve.wait_ge(router_hi_done, 1)
                    nc.vector.tensor_tensor(s2_lo[:, :, ER:ER + NR], router_raw[:, :, :], s2_hi[:, :, ER:ER + NR],
                                            ALU.subtract).then_inc(router_lo_done, 1)
            for c in range(5, N_SHARED - 1):
                shared_lo(c)
            dve.wait_ge(small_in, 48)
            nc.vector.tensor_copy(map_f[:, :], map_i[:, :]).then_inc(mask_done, 1)
            dve.wait_ge(mask_done, 1)
            for e in range(E):
                nc.vector.tensor_scalar(expert_mask[:, e, :], map_f[:, :], float(e), None, ALU.is_equal).then_inc(mask_done, 1)
            dve.wait_ge(mask_done, 1 + E)
            routing(0)
            shared_lo(N_SHARED - 1)
            x_lo(0, 0)
            make_hwt_lo(0)
            x_lo(0, 1)
            for o in range(OC, OC + W_SLOTS - 1):
                adapter_lo(0, o)
            add_bias(0)
            output(0)

            with dve.Fori(1, NB - 1) as b:
                element(b)
            element(NB - 1, last=True)

        @block.tensor
        def _(pe):
            def stage1_chunk(b, o):
                slot = o % W_SLOTS
                pe.wait_ge(w_lo_done, split(b, o))
                pe.wait_ge(y_sum_done, OC * b + o - 1)
                for k in range(KC):
                    nc.tensor.matmul(y_ps[:, o % 2, :], w_hi[:, slot, k, :],
                                     x_split[:, k, :, :].rearrange("p s t -> p (s t)"), start=(k == 0), stop=False)
                    mm = nc.tensor.matmul(y_ps[:, o % 2, 0:T], w_lo[:, slot, k, :], x_split[:, k, 0, :],
                                          start=False, stop=(k == KC - 1))
                mm.then_inc(y_ps_done, 1)

            def stage1_float32(o):
                if o > 0:
                    pe.wait_ge(w_in[o], 16)
                for k in range(KC):
                    if o == 0 and k % KP == 0:
                        pe.wait_ge(x0_in[k // KP], 16)
                        pe.wait_ge(w0_in[k // KP], 16)
                    mm = nc.tensor.matmul(y_ps[:, o, 0:T], w_raw[:, o, k, :], x_raw[:, k, :], start=(k == 0), stop=(k == KC - 1))
                mm.then_inc(y_ps_done, 1)

            def group(b, t, g, first=False, y_fresh=False):
                if not first:
                    pe.wait_ge(out_done, NG * (NT * (b - 1) + t) + g + 1)
                cols = slice(EDGE[g], EDGE[g + 1])
                dst = s2_ps[:, g, t, 0:EDGE[g + 1] - EDGE[g]]
                for k in range(KC):
                    if first and t == 0:
                        for c, (part, ks) in enumerate(PARTS):
                            if part == g and k == ks.start:
                                pe.wait_ge(c_lo_done, c + 2)
                    if y_fresh and k >= KC - 2:
                        pe.wait_ge(y_lo_done, OC * b + k + 1)
                    hi, lo = (y[:, k, t * P:(t + 1) * P] for y in (y_hi, y_lo))
                    nc.tensor.matmul(dst, hi, s2_hi[:, k, cols], start=(k == 0), stop=False)
                    nc.tensor.matmul(dst, hi, s2_lo[:, k, cols], start=False, stop=False)
                    mm = nc.tensor.matmul(dst, lo, s2_hi[:, k, cols], start=False, stop=(g == 0 and k == KC - 1))
                return mm

            def lora_b(t, g):
                dst = s2_ps[:, g, t, (AR if g == 0 else 0):EDGE[g + 1] - EDGE[g]]
                cols = slice(OUT[g], OUT[g + 1])
                skip = g == 0
                nc.tensor.matmul(dst, hwt_hi[:, t, :], b_hi[:, cols], start=False, stop=False, skip_group_check=skip)
                nc.tensor.matmul(dst, hwt_hi[:, t, :], b_lo[:, cols], start=False, stop=False, skip_group_check=skip)
                nc.tensor.matmul(dst, hwt_lo[:, t, :], b_hi[:, cols], start=False, stop=True,
                                 skip_group_check=skip).then_inc(s2_ps_done, 1)

            def stage2(b, first=False):
                if first:
                    pe.wait_ge(router_lo_done, 1)
                    pe.wait_ge(pad_done, 2)
                pe.wait_ge(y_lo_done, OC * b + OC - 2)
                group(b, 0, 0, first, y_fresh=True)
                group(b, 1, 0, first).then_inc(ar_done, 1)
                group(b, 0, 1, first)
                group(b, 0, 2, first)
                pe.wait_ge(hw_done, b + 1)
                for t in range(NT):
                    mm = nc.tensor.matmul(s2_ps[:, 0, t, HWT:HWT + P], hw[:, t, :], ident[:, :], is_transpose=True,
                                          start=False, stop=True, skip_group_check=True)
                mm.then_inc(hwt_done, 1)
                group(b, 1, 1, first)
                if first:
                    pe.wait_ge(c_lo_done, N_SHARED)
                pe.wait_ge(hwt_lo_done, b + 1)
                for g in range(NG):
                    lora_b(0, g)
                for g in range(NG - 1):
                    lora_b(1, g)
                group(b, 1, 2, first).then_inc(y_free, 1)
                lora_b(1, 2)

            def element(b):
                pe.wait_ge(x_lo_done, 2 * b)
                for o in range(OC):
                    stage1_chunk(b, o)
                stage2(b)

            pe.wait_ge(ident_done, 2)
            for i in range(WARM_UP):
                nc.tensor.matmul(s2_ps[:, 2, 1, 0:P], ident[:, :], ident[:, :], start=True, stop=True)
            for o in range(F32_CHUNKS):
                stage1_float32(o)
            pe.wait_ge(x0_lo_done, PIECES)
            for o in range(F32_CHUNKS, OC):
                stage1_chunk(0, o)
            stage2(0, first=True)

            with pe.Fori(1, NB - 1) as b:
                element(b)
            element(NB - 1)

        @block.gpsimd
        def _(pool):
            nc.gpsimd.memset(ident[:, :], 0.0).then_inc(ident_done, 1)
            pool.wait_ge(ident_done, 1)
            nc.gpsimd.affine_select(out=ident[:, :], in_=ident[:, :], compare_op=ALU.not_equal, fill=1.0, base=0,
                                    pattern=[[-1, P]], channel_multiplier=1).then_inc(ident_done, 1)
            nc.gpsimd.memset(s2_hi[:, :, AR - 1:AR].bitcast(F32), 0.0).then_inc(pad_done, 1)
            nc.gpsimd.memset(s2_lo[:, :, AR - 1:AR].bitcast(F32), 0.0).then_inc(pad_done, 1)


def kernel(x, itok_B_3_7, L0_cond_weight, L0_ffn_base_W, L0_ffn_base_b, L0_ffn_router_W, L0_ffn_router_b,
           L0_ffn_A, L0_ffn_B, L0_ffn_expert_map):
    import numpy as np
    import concourse.bacc as bacc
    from concourse.bass_utils import run_bass_kernel_spmd

    nc = bacc.Bacc("TRN2", target_bir_lowering=False, num_devices=1)
    NB, T, D = x.shape
    NA = L0_cond_weight.shape[0]
    E, R, _ = L0_ffn_A.shape
    NR = L0_ffn_router_W.shape[0]
    KC = D // P
    x, cond, base, a, bm, router = (np.asarray(v) for v in (x, L0_cond_weight, L0_ffn_base_W, L0_ffn_A, L0_ffn_B, L0_ffn_router_W))
    arrays = {
        "xT": x.reshape(NB, T, KC, P).transpose(0, 3, 2, 1),
        "x": x,
        "ids": np.asarray(itok_B_3_7).reshape(1, NB),
        "wT": cond.reshape(NA, KC, P, KC, P).transpose(0, 1, 4, 3, 2),
        "a_t": a.reshape(E * R, KC, P).transpose(2, 1, 0),
        "base_t": base.reshape(D, KC, P).transpose(2, 1, 0),
        "b_t": bm.transpose(0, 2, 1).reshape(E * R, D),
        "router_t": router.reshape(NR, KC, P).transpose(2, 1, 0),
        "base_b": np.asarray(L0_ffn_base_b),
        "router_b": np.asarray(L0_ffn_router_b),
        "expert_map": np.asarray(L0_ffn_expert_map),
    }
    arrays = {name: np.ascontiguousarray(v) for name, v in arrays.items()}
    args = [nc.dram_tensor(f"in_{name}", v.shape, mybir.dt.from_np(v.dtype), kind="ExternalInput").ap() for name, v in arrays.items()]
    args.append(nc.dram_tensor("out", (NB, T, D), F32, kind="ExternalOutput").ap())
    adaln_ffn_kernel(nc, *args)
    result = run_bass_kernel_spmd(nc, [{f"in_{name}": v for name, v in arrays.items()}], core_ids=[0])
    return result.results[0]["out"]
```
